# Optimizing a Trainium2 kernel written in Bass

```python
import numpy as np
import jax
import jax.numpy as jnp

def _softmax(x, axis=-1):
    return jax.nn.softmax(x, axis=axis)

def _gelu(x):
    return jax.nn.gelu(x, approximate=True)

def _silu(x):
    return jax.nn.silu(x)

def _sigmoid(x):
    return jax.nn.sigmoid(x)

def _layernorm(x, axis=-1, eps=1e-05):
    m = jnp.mean(x, axis=axis, keepdims=True)
    v = jnp.var(x, axis=axis, keepdims=True)
    return (x - m) / jnp.sqrt(v + eps)

def _scatter_add(tgt, idx, src, axis=0):
    return tgt.at[idx].add(src)

def _segment_sum(src, seg, n):
    return jax.ops.segment_sum(src, seg, n)
kernel_name = 'mk_xattn_seq_d1_seqx_r4_fa4a87'

def setup_inputs(seed: int=0):
    np.random.seed(seed)
    _w = jnp.asarray

    def _rec_inputs():
        import jax
        import jax.numpy as jnp
        _rk = jax.random.key(seed)
        x = -0.000125 + 0.9999 * jax.random.normal(jax.random.fold_in(_rk, 1), (16, 128, 1024), jnp.float32)
        _lenS = 128 - jax.random.randint(jax.random.fold_in(_rk, 7), (16,), 0, max(1, 128 // 4) + 1, jnp.int32)
        _lenS2 = 128 - jax.random.randint(jax.random.fold_in(_rk, 8), (16,), 0, max(1, 128 // 4) + 1, jnp.int32)
        _ctx_4096P = jax.random.normal(jax.random.fold_in(_rk, 11), (16, 16, 1024), jnp.float32)
        _ctx_4096c = jax.random.dirichlet(jax.random.fold_in(_rk, 511), 0.3 * jnp.ones((16,), jnp.float32), (16, 128))
        _ctx_4096t = jnp.einsum('bsk,bkd->bsd', _ctx_4096c, _ctx_4096P)
        _ctx_4096t = _ctx_4096t * jax.lax.rsqrt(jnp.mean(jnp.square(_ctx_4096t)) + 1e-12) * 0.953939
        ctx_4096 = -1.52775e-05 + 0.999936 * (_ctx_4096t + 0.3 * jax.random.normal(jax.random.fold_in(_rk, 611), (16, 128, 1024), jnp.float32))
        return (x, ctx_4096)
    x, ctx_4096 = _rec_inputs()

    def _L0_xattn_setup():
        import jax, jax.numpy as jnp
        import numpy as np
        B, C, N, H = (16, 128, 1024, 8)
        key = jax.random.key(seed)
        ks = jax.random.split(key, 10)
        s = 0.02
        return {'rgb_emb': jax.random.normal(ks[0], (B, C, N), jnp.float32), 'geo_emb': jax.random.normal(ks[1], (B, C, N), jnp.float32), 'wq_rgb': jax.random.normal(ks[2], (C, C), jnp.float32) * s, 'wk_rgb': jax.random.normal(ks[3], (C, C), jnp.float32) * s, 'wv_rgb': jax.random.normal(ks[4], (C, C), jnp.float32) * s, 'wq_point': jax.random.normal(ks[5], (C, C), jnp.float32) * s, 'wk_point': jax.random.normal(ks[6], (C, C), jnp.float32) * s, 'wv_point': jax.random.normal(ks[7], (C, C), jnp.float32) * s, 'proj_r2p': jax.random.normal(ks[8], (C, C), jnp.float32) * s, 'proj_p2r': jax.random.normal(ks[9], (C, C), jnp.float32) * s}
    _L0_xattn_all = _L0_xattn_setup()
    _L0_xattn_in = {k: v for k, v in _L0_xattn_all.items() if k in ('wq_rgb', 'wk_rgb', 'wv_rgb', 'wq_point', 'wk_point', 'wv_point', 'proj_r2p', 'proj_p2r')}
    del _L0_xattn_all
    return {'x': x, 'ctx_4096': ctx_4096, 'L0_xattn_wq_rgb': _L0_xattn_in['wq_rgb'], 'L0_xattn_wk_rgb': _L0_xattn_in['wk_rgb'], 'L0_xattn_wv_rgb': _L0_xattn_in['wv_rgb'], 'L0_xattn_wq_point': _L0_xattn_in['wq_point'], 'L0_xattn_wk_point': _L0_xattn_in['wk_point'], 'L0_xattn_wv_point': _L0_xattn_in['wv_point'], 'L0_xattn_proj_r2p': _L0_xattn_in['proj_r2p'], 'L0_xattn_proj_p2r': _L0_xattn_in['proj_p2r']}

def reference(x, ctx_4096, L0_xattn_wq_rgb, L0_xattn_wk_rgb, L0_xattn_wv_rgb, L0_xattn_wq_point, L0_xattn_wk_point, L0_xattn_wv_point, L0_xattn_proj_r2p, L0_xattn_proj_p2r):
    import jax
    import jax.numpy as jnp

    def _L0_xattn_ref(rgb_emb, geo_emb, wq_rgb, wk_rgb, wv_rgb, wq_point, wk_point, wv_point, proj_r2p, proj_p2r):
        import jax, jax.numpy as jnp
        import numpy as np
        B, C, N, H = (16, 128, 1024, 8)
        rgb = jnp.transpose(rgb_emb, (0, 2, 1))
        geo = jnp.transpose(geo_emb, (0, 2, 1))
        b, n, c = rgb.shape
        d = c // H
        scale = d ** (-0.5)

        def heads(x, w):
            return (x @ w.T).reshape(b, n, H, d).transpose(0, 2, 1, 3)

        def xca(q, k, v):
            attn = jax.nn.softmax(jnp.einsum('bhni,bhnj->bhij', q, k) * scale, axis=-1)
            out = jnp.einsum('bhnd,bhde->bhne', v, attn)
            return out.transpose(0, 2, 1, 3).reshape(b, n, c)
        res_p2r = xca(heads(rgb, wq_rgb), heads(geo, wk_point), heads(geo, wv_point)) @ proj_p2r.T
        res_r2p = xca(heads(geo, wq_point), heads(rgb, wk_rgb), heads(rgb, wv_rgb)) @ proj_r2p.T
        rgb_att = jnp.transpose(rgb + res_p2r, (0, 2, 1))
        geo_att = jnp.transpose(geo + res_r2p, (0, 2, 1))
        return rgb_att + geo_att
    x = _L0_xattn_ref(x, ctx_4096, L0_xattn_wq_rgb, L0_xattn_wk_rgb, L0_xattn_wv_rgb, L0_xattn_wq_point, L0_xattn_wk_point, L0_xattn_wv_point, L0_xattn_proj_r2p, L0_xattn_proj_p2r)
    return x

_drawn_inputs = setup_inputs


def setup_inputs(seed=0):
    import zlib

    import numpy as np

    out = dict(_drawn_inputs(seed))
    spreads = {}
    factors = {'L0_xattn_wq_rgb': 8.0,
     'L0_xattn_wk_rgb': 8.0,
     'L0_xattn_wv_rgb': 5.733,
     'L0_xattn_wq_point': 8.0,
     'L0_xattn_wk_point': 8.0,
     'L0_xattn_wv_point': 6.041,
     'L0_xattn_proj_r2p': 5.559,
     'L0_xattn_proj_p2r': 5.836}
    for name, (base, spread) in spreads.items():
        noise = np.random.default_rng([zlib.crc32(name.encode()), seed]).standard_normal(out[name].shape)
        drawn = base * np.exp(spread * noise) if base else spread * noise
        out[name] = jnp.asarray(drawn.astype(out[name].dtype))
    for name, factor in factors.items():
        out[name] = (out[name] * factor).astype(out[name].dtype)
    return out
```

```python
from contextlib import ExitStack

import concourse.bass as bass
from concourse import mybir

F32 = mybir.dt.float32
F32R = mybir.dt.float32r
ALU = mybir.AluOpType
ACT = mybir.ActivationFunctionType

P = 128
HEADS = 8
TILE = 128
BANK = 512
SLOTS = 4
OUT_SLOTS = 2
OFF_HEAD = -3.0e38


def bass_cross_channel_attention(nc: bass.Bass, x, ctx, wq_rgb, wk_rgb, wv_rgb, wq_point, wk_point, wv_point,
                                 proj_r2p, proj_p2r, out):
    B, C, N = x.shape
    D = C // HEADS
    SCALE = float(D) ** -0.5
    HALF = N // 2
    TILES = N // TILE
    assert C == P and HALF == BANK and B % SLOTS == 0 and B >= 3 * SLOTS

    with ExitStack() as stack:
        def sb(name, shape, dt=F32):
            return stack.enter_context(nc.sbuf_tensor(name, shape, dt))

        def psum(name, shape):
            return stack.enter_context(nc.psum_tensor(name, shape, F32))

        def sem(name):
            return stack.enter_context(nc.semaphore(name))

        x_raw = sb("x_raw", [P, SLOTS, N])
        g_raw = sb("g_raw", [P, SLOTS, N])
        x_hi = sb("x_hi", [P, SLOTS, N], F32R)
        x_lo = sb("x_lo", [P, SLOTS, N], F32R)
        g_hi = sb("g_hi", [P, SLOTS, N], F32R)
        g_lo = sb("g_lo", [P, SLOTS, N], F32R)
        out_sb = sb("out_sb", [P, OUT_SLOTS, N])
        xt = sb("xt", [P, N])
        gt = sb("gt", [P, N])
        gram = sb("gram", [P, P])
        uv = sb("uv", [P, 2, P])
        scores = sb("scores", [P, 2, P])
        min_neg = sb("min_neg", [P, 2])
        expd = sb("expd", [P, 2, P])
        row_sum = sb("row_sum", [P, 2])
        row_inv = sb("row_inv", [P, 2])
        probs = sb("probs", [P, 2, P])
        y_sb = sb("y_sb", [P, 2, P])
        t_sb = sb("t_sb", [P, 2, P])
        t_hi = sb("t_hi", [P, 2, P], F32R)
        t_lo = sb("t_lo", [P, 2, P], F32R)
        WQR, WKR, WKP, WQP, PP, PR, WVP, WVR = range(8)
        w_raw = sb("w_raw", [P, 8, P])
        w_t = sb("w_t", [P, 6, P])
        ident = sb("ident", [P, P])
        ident2 = sb("ident2", [P, 2, P])
        head_mask = sb("head_mask", [P, P])

        xt_ps = psum("xt_ps", [P, N])
        gt_ps = psum("gt_ps", [P, N])
        out_ps = psum("out_ps", [P, N])
        gu_ps = psum("gu_ps", [P, BANK])
        sy_ps = psum("sy_ps", [P, BANK])
        gram_ps = gu_ps[:, 0:P]
        uv_ps = gu_ps[:, P:3 * P]
        s_ps = sy_ps[:, 0:2 * P]
        t_ps = sy_ps[:, 0:2 * P]
        y_ps = sy_ps[:, 2 * P:4 * P]

        x_loaded = [sem(f"x_loaded{s}") for s in range(SLOTS)]
        g_loaded = [sem(f"g_loaded{s}") for s in range(SLOTS)]
        out_stored = [sem(f"out_stored{s}") for s in range(OUT_SLOTS)]
        w_loaded = sem("w_loaded")
        ident_ready = sem("ident_ready")
        ident2_ready = sem("ident2_ready")
        mask_ready = sem("mask_ready")
        w_turned = sem("w_turned")
        w_ready = sem("w_ready")
        xt_done = sem("xt_done")
        gt_done = sem("gt_done")
        xt_copied = sem("xt_copied")
        gt_copied = sem("gt_copied")
        gram_done = sem("gram_done")
        gram_copied = sem("gram_copied")
        uv_done = sem("uv_done")
        uv_copied = sem("uv_copied")
        s_done = sem("s_done")
        s_masked = sem("s_masked")
        exp_done = sem("exp_done")
        inv_done = sem("inv_done")
        probs_ready = sem("probs_ready")
        y_done = sem("y_done")
        y_copied = sem("y_copied")
        t_done = sem("t_done")
        t_summed = sem("t_summed")
        t_hi_ready = sem("t_hi_ready")
        t_lo_ready = sem("t_lo_ready")
        x_hi_ready = sem("x_hi_ready")
        g_hi_ready = sem("g_hi_ready")
        lo_ready = sem("lo_ready")
        half_done = sem("half_done")
        half_copied = sem("half_copied")

        block = stack.enter_context(nc.Block())

        def steps(eng, step, first, last):
            whole = range(SLOTS, last + 1 - (last + 1) % SLOTS)
            for i in range(first, whole.start):
                step(i, i % SLOTS, i // SLOTS, i)
            with eng.Fori(whole.start // SLOTS, whole.stop // SLOTS) as t:
                for slot in range(SLOTS):
                    step(t * SLOTS + slot, slot, t, SLOTS + slot)
            for i in range(whole.stop, last + 1):
                step(i, i % SLOTS, i // SLOTS, i)

        @block.gpsimd
        def _(pool):
            nc.gpsimd.memset(ident[:, :], 0.0).then_inc(ident_ready, 1)
            pool.wait_ge(ident_ready, 1)
            nc.gpsimd.affine_select(out=ident[:, :], in_=ident[:, :], compare_op=ALU.not_equal, fill=1.0, base=0,
                                    pattern=[[-1, P]], channel_multiplier=1).then_inc(ident_ready, 1)
            nc.gpsimd.memset(head_mask[:, :], 0.0).then_inc(mask_ready, 1)
            pool.wait_ge(mask_ready, 1)
            mask = head_mask[:, :].rearrange("p (h d) -> p h d", h=HEADS)
            nc.gpsimd.affine_select(out=mask, in_=mask, compare_op=ALU.is_ge, fill=OFF_HEAD, base=0,
                                    pattern=[[-D, HEADS], [0, D]], channel_multiplier=1).then_inc(mask_ready, 1)
            pool.wait_ge(mask_ready, 2)
            nc.gpsimd.affine_select(out=mask, in_=mask, compare_op=ALU.is_ge, fill=OFF_HEAD, base=D - 1,
                                    pattern=[[D, HEADS], [0, D]], channel_multiplier=-1).then_inc(mask_ready, 1)
            pool.wait_ge(ident_ready, 2)
            nc.gpsimd.tensor_copy(ident2[:, 0, :], ident[:, :]).then_inc(ident2_ready, 1)
            nc.gpsimd.tensor_copy(ident2[:, 1, :], ident[:, :]).then_inc(ident2_ready, 1)

        @block.sync
        def _(sp):
            def load(b, slot):
                sp.dma_start(x_raw[:, slot, :], x[b]).then_inc(x_loaded[slot], 16)
                sp.dma_start(g_raw[:, slot, :], ctx[b]).then_inc(g_loaded[slot], 16)

            def store(b, slot):
                sp.wait_ge(half_copied, 2 * b + 2)
                sp.dma_start(out[b], out_sb[:, slot % OUT_SLOTS, :]).then_inc(out_stored[slot % OUT_SLOTS], 16)

            def reload(i, slot):
                sp.wait_ge(xt_done, 2 * i + 2)
                sp.wait_ge(gt_done, 2 * i + 2)
                sp.wait_ge(lo_ready, 2 * i + 2)
                load(i + SLOTS, slot)

            def step(i, slot, visit, i_min):
                reload(i, slot)
                if i_min >= 2:
                    store(i - 2, slot)

            for b in range(SLOTS):
                load(b, b)
            steps(sp, step, 0, B - SLOTS - 1)
            for b in range(B - SLOTS - 2, B):
                store(b, b % SLOTS)
            for s in range(OUT_SLOTS):
                sp.wait_ge(out_stored[s], 16 * (B // OUT_SLOTS))

        @block.tensor
        def _(pe):
            pe.wait_ge(ident_ready, 2)
            pe.wait_ge(w_loaded, 16 * 8)
            for w in range(6):
                last = nc.tensor.transpose(out_ps[:, w * P:(w + 1) * P], w_raw[:, w, :], ident[:, :])
            last.then_inc(w_turned, 1)

            def turn(i, visit, i_min, half, raw, slot, loaded, ps, done, copied):
                if half == 0:
                    pe.wait_ge(loaded[slot], 16 * visit + 16)
                if i_min >= 1:
                    pe.wait_ge(copied, 2 * i - 1 + half)
                for t in range(half * TILES // 2, (half + 1) * TILES // 2):
                    cols = slice(t * TILE, (t + 1) * TILE)
                    last = nc.tensor.transpose(ps[:, cols], raw[:, slot, cols], ident[:, :])
                last.then_inc(done, 1)

            def gram_half(i, half, i_min):
                pe.wait_ge(xt_copied, 2 * i + 1 + half)
                pe.wait_ge(gt_copied, 2 * i + 1 + half)
                if half == 0 and i_min >= 1:
                    pe.wait_ge(gram_copied, i)
                for t in range(half * TILES // 2, (half + 1) * TILES // 2):
                    cols = slice(t * TILE, (t + 1) * TILE)
                    last = nc.tensor.matmul(gram_ps, xt[:, cols], gt[:, cols], start=(t == 0), stop=(t == TILES - 1))
                if half == 1:
                    last.then_inc(gram_done, 1)

            def last_half(b, slot, half, b_min):
                cols = slice(half * HALF, (half + 1) * HALF)
                if b_min >= 1:
                    pe.wait_ge(half_copied, 2 * b - 1 + half)
                parts = [(t_hi, 0, x_hi), (t_lo, 0, x_hi), (t_hi, 0, x_lo), (t_hi, 1, g_hi), (t_lo, 1, g_hi), (t_hi, 1, g_lo)]
                for n, (w, which, moving) in enumerate(parts):
                    last = nc.tensor.matmul(out_ps[:, cols], w[:, which, :], moving[:, slot, cols],
                                            start=(n == 0), stop=(n == len(parts) - 1))
                last.then_inc(half_done, 1)

            def step(i, slot, visit, i_min):
                gram_on, small_on, last_on = i_min < B, 1 <= i_min <= B, i_min >= 2
                before = (slot - 2) % SLOTS
                if gram_on:
                    turn(i, visit, i_min, 0, x_raw, slot, x_loaded, xt_ps, xt_done, xt_copied)
                    turn(i, visit, i_min, 0, g_raw, slot, g_loaded, gt_ps, gt_done, gt_copied)
                if small_on:
                    pe.wait_ge(gram_copied, i)
                    if i_min == 1:
                        pe.wait_ge(w_ready, 1)
                    else:
                        pe.wait_ge(uv_copied, i - 1)
                    nc.tensor.matmul(uv_ps, gram[:, :], w_t[:, WQR:WKR + 1, :], start=True,
                                     stop=True).then_inc(uv_done, 1)
                if gram_on:
                    turn(i, visit, i_min, 1, x_raw, slot, x_loaded, xt_ps, xt_done, xt_copied)
                    turn(i, visit, i_min, 1, g_raw, slot, g_loaded, gt_ps, gt_done, gt_copied)
                if small_on:
                    pe.wait_ge(uv_copied, i)
                    if i_min >= 2:
                        pe.wait_ge(t_summed, i - 1)
                    nc.tensor.matmul(s_ps[:, 0:P], uv[:, 0, :], w_t[:, WKP, :], start=True, stop=True)
                    nc.tensor.matmul(s_ps[:, P:2 * P], w_t[:, WQP, :], uv[:, 1, :], start=True,
                                     stop=True).then_inc(s_done, 1)
                if gram_on:
                    gram_half(i, 0, i_min)
                if last_on:
                    pe.wait_ge(t_lo_ready, i - 1)
                    pe.wait_ge(lo_ready, 2 * i - 2)
                    last_half(i - 2, before, 0, i_min - 2)
                if gram_on:
                    gram_half(i, 1, i_min)
                if small_on:
                    pe.wait_ge(probs_ready, 2 * i)
                    if i_min >= 2:
                        pe.wait_ge(y_copied, i - 1)
                    for a, wv in enumerate((WVP, WVR)):
                        last = nc.tensor.matmul(y_ps[:, a * P:(a + 1) * P], probs[:, a, :], w_raw[:, wv, :],
                                                start=True, stop=True)
                    last.then_inc(y_done, 1)
                if last_on:
                    last_half(i - 2, before, 1, i_min - 2)
                if small_on:
                    pe.wait_ge(y_copied, i)
                    nc.tensor.matmul(t_ps[:, 0:P], y_sb[:, 1, :], w_t[:, PR, :], start=True, stop=True)
                    nc.tensor.matmul(t_ps[:, P:2 * P], y_sb[:, 0, :], w_t[:, PP, :], start=True,
                                     stop=True).then_inc(t_done, 1)

            steps(pe, step, 0, B + 1)

        @block.scalar
        def _(act):
            for w, src in enumerate((wq_rgb, wk_rgb, wk_point, wq_point, proj_p2r, proj_r2p, wv_point, wv_rgb)):
                act.dma_start(w_raw[:, w, :], src).then_inc(w_loaded, 16)
            act.wait_ge(w_turned, 1)
            nc.scalar.copy(w_t[:, :, :], out_ps[:, 0:6 * P].rearrange("p (w c) -> p w c", w=6)).then_inc(w_ready, 1)

            def copy_xt(i, half, i_min):
                act.wait_ge(xt_done, 2 * i + 1 + half)
                if i_min >= 1:
                    act.wait_ge(gram_done, i)
                cols = slice(half * HALF, (half + 1) * HALF)
                nc.scalar.copy(xt[:, cols], xt_ps[:, cols]).then_inc(xt_copied, 1)

            def split_hi(i, slot, visit, i_min, raw, hi, loaded, ready):
                act.wait_ge(loaded[slot], 16 * visit + 16)
                if i_min >= SLOTS:
                    act.wait_ge(half_done, 2 * i - 6)
                nc.scalar.copy(hi[:, slot, :], raw[:, slot, :]).then_inc(ready, 1)

            def step(i, slot, visit, i_min):
                gram_on, small_on, last_on = i_min < B, 1 <= i_min <= B, i_min >= 2
                if gram_on:
                    copy_xt(i, 0, i_min)
                if last_on:
                    act.wait_ge(t_summed, i - 1)
                    if i_min >= 3:
                        act.wait_ge(half_done, 2 * i - 4)
                    nc.scalar.copy(t_hi[:, :, :], t_sb[:, :, :]).then_inc(t_hi_ready, 1)
                if small_on:
                    act.wait_ge(uv_done, i)
                    if i_min >= 2:
                        act.wait_ge(s_done, i - 1)
                    nc.scalar.copy(uv[:, :, :], uv_ps.rearrange("p (a c) -> p a c", a=2)).then_inc(uv_copied, 1)
                if gram_on:
                    copy_xt(i, 1, i_min)
                    split_hi(i, slot, visit, i_min, x_raw, x_hi, x_loaded, x_hi_ready)
                if small_on:
                    if i_min >= 2:
                        act.wait_ge(probs_ready, 2 * i - 2)
                    for a in range(2):
                        act.wait_ge(s_masked, 2 * i - 1 + a)
                        nc.scalar.activation(expd[:, a, :], scores[:, a, :], ACT.Exp, bias=min_neg[:, a:a + 1], scale=-1.0,
                                             accum_out=row_sum[:, a:a + 1]).then_inc(exp_done, 1)
                if gram_on:
                    split_hi(i, slot, visit, i_min, g_raw, g_hi, g_loaded, g_hi_ready)
                if last_on:
                    for half in range(2):
                        act.wait_ge(half_done, 2 * i - 3 + half)
                        if half == 0 and i_min >= 4:
                            act.wait_ge(out_stored[slot % OUT_SLOTS], 16 * (visit * 2 + slot // 2 - 1))
                        cols = slice(half * HALF, (half + 1) * HALF)
                        nc.scalar.copy(out_sb[:, slot % OUT_SLOTS, cols], out_ps[:, cols]).then_inc(half_copied, 1)

            steps(act, step, 0, B + 1)

        @block.vector
        def _(dve):
            def copy_gt(i, half, i_min):
                dve.wait_ge(gt_done, 2 * i + 1 + half)
                if i_min >= 1:
                    dve.wait_ge(gram_done, i)
                cols = slice(half * HALF, (half + 1) * HALF)
                nc.vector.tensor_copy(gt[:, cols], gt_ps[:, cols]).then_inc(gt_copied, 1)

            def split_lo(i, slot, i_min, raw, hi, lo, hi_ready):
                dve.wait_ge(hi_ready, i + 1)
                nc.vector.tensor_tensor(lo[:, slot, :], raw[:, slot, :], hi[:, slot, :].bitcast(F32),
                                        ALU.subtract).then_inc(lo_ready, 1)

            dve.wait_ge(ident2_ready, 2)

            def step(i, slot, visit, i_min):
                gram_on, small_on, last_on = i_min < B, 1 <= i_min <= B, i_min >= 2
                if last_on:
                    dve.wait_ge(t_done, i - 1)
                    if i_min >= 3:
                        dve.wait_ge(t_lo_ready, i - 2)
                    nc.vector.tensor_tensor(t_sb[:, :, :], t_ps.rearrange("p (a c) -> p a c", a=2), ident2[:, :, :],
                                            ALU.add).then_inc(t_summed, 1)
                if gram_on:
                    copy_gt(i, 0, i_min)
                if last_on:
                    dve.wait_ge(t_hi_ready, i - 1)
                    if i_min >= 3:
                        dve.wait_ge(half_done, 2 * i - 4)
                    nc.vector.tensor_tensor(t_lo[:, :, :], t_sb[:, :, :], t_hi[:, :, :].bitcast(F32),
                                            ALU.subtract).then_inc(t_lo_ready, 1)
                if gram_on:
                    copy_gt(i, 1, i_min)
                if small_on:
                    dve.wait_ge(mask_ready, 3)
                    dve.wait_ge(s_done, i)
                    for a in range(2):
                        nc.vector.tensor_tensor_reduce(out=scores[:, a, :], in0=s_ps[:, a * P:(a + 1) * P],
                                                       in1=head_mask[:, :], scale=-SCALE, scalar=3.0e38, op0=ALU.add,
                                                       op1=ALU.min, accum_out=min_neg[:, a:a + 1]).then_inc(s_masked, 1)
                if gram_on:
                    split_lo(i, slot, i_min, x_raw, x_hi, x_lo, x_hi_ready)
                if small_on:
                    dve.wait_ge(exp_done, 2 * i)
                    nc.vector.reciprocal(row_inv[:, :], row_sum[:, :]).then_inc(inv_done, 1)
                    dve.wait_ge(inv_done, i)
                    if i_min >= 2:
                        dve.wait_ge(y_done, i - 1)
                    for a in range(2):
                        nc.vector.tensor_scalar(probs[:, a, :], expd[:, a, :], row_inv[:, a:a + 1], None,
                                                ALU.mult).then_inc(probs_ready, 1)
                if gram_on:
                    split_lo(i, slot, i_min, g_raw, g_hi, g_lo, g_hi_ready)
                    dve.wait_ge(gram_done, i + 1)
                    if i_min >= 1:
                        dve.wait_ge(uv_done, i)
                    nc.vector.tensor_copy(gram[:, :], gram_ps).then_inc(gram_copied, 1)
                if small_on:
                    dve.wait_ge(y_done, i)
                    if i_min >= 2:
                        dve.wait_ge(t_done, i - 1)
                    nc.vector.tensor_copy(y_sb[:, :, :], y_ps.rearrange("p (a c) -> p a c", a=2)).then_inc(y_copied, 1)

            steps(dve, step, 0, B + 1)


_INS = ['x', 'ctx_4096', 'L0_xattn_wq_rgb', 'L0_xattn_wk_rgb', 'L0_xattn_wv_rgb', 'L0_xattn_wq_point',
        'L0_xattn_wk_point', 'L0_xattn_wv_point', 'L0_xattn_proj_r2p', 'L0_xattn_proj_p2r']


def kernel(**inputs):
    import numpy as _np
    import concourse.bacc as _bacc
    from concourse import mybir as _mybir
    from concourse.bass_utils import run_bass_kernel_spmd as _run

    nc = _bacc.Bacc("TRN2", target_bir_lowering=False, num_devices=1)
    arrays, args = {}, []
    for name in _INS:
        a = _np.ascontiguousarray(inputs[name])
        arrays[f"in_{name}_dram"] = a
        args.append(nc.dram_tensor(f"in_{name}_dram", a.shape, _mybir.dt.from_np(a.dtype), kind="ExternalInput").ap())
    shape = arrays["in_x_dram"].shape
    args.append(nc.dram_tensor("out_0_dram", shape, _mybir.dt.float32, kind="ExternalOutput").ap())
    bass_cross_channel_attention(nc, *args)
    r = _run(nc, [arrays], core_ids=[0])
    return r.results[0]["out_0_dram"]
```

```python
from contextlib import ExitStack

import concourse.bass as bass
from concourse import mybir

F32 = mybir.dt.float32
F32R = mybir.dt.float32r
ALU = mybir.AluOpType
ACT = mybir.ActivationFunctionType

P = 128
HEADS = 8
TILE = 128
BANK = 512
SLOTS = 4
OUT_SLOTS = 2
OFF_HEAD = -3.0e38
WARM = 24


WQR, WKR, WKP, WQP, PP, PR, WVP, WVR = range(8)


def bass_cross_channel_attention(nc: bass.Bass, x, ctx, weights, out):
    B, C, N = x.shape
    D = C // HEADS
    SCALE = float(D) ** -0.5
    HALF = N // 2
    TILES = N // TILE
    assert C == P and HALF == BANK and B % SLOTS == 0 and B >= 3 * SLOTS

    with ExitStack() as stack:
        def sb(name, shape, dt=F32):
            return stack.enter_context(nc.sbuf_tensor(name, shape, dt))

        def psum(name, shape):
            return stack.enter_context(nc.psum_tensor(name, shape, F32))

        def sem(name):
            return stack.enter_context(nc.semaphore(name))

        x_raw = sb("x_raw", [P, SLOTS, N])
        g_raw = sb("g_raw", [P, SLOTS, N])
        x_hi = sb("x_hi", [P, SLOTS, N], F32R)
        x_lo = sb("x_lo", [P, SLOTS, N], F32R)
        g_hi = sb("g_hi", [P, SLOTS, N], F32R)
        g_lo = sb("g_lo", [P, SLOTS, N], F32R)
        out_sb = sb("out_sb", [P, OUT_SLOTS, N])
        xt = sb("xt", [P, N])
        gt = sb("gt", [P, N])
        gram_hi = sb("gram_hi", [P, P], F32R)
        gram_lo = sb("gram_lo", [P, P], F32R)
        uv = sb("uv", [P, 2, P])
        scores = sb("scores", [P, 2, P])
        min_neg = sb("min_neg", [P, 2])
        expd = sb("expd", [P, 2, P])
        row_sum = sb("row_sum", [P, 2])
        row_inv = sb("row_inv", [P, 2])
        probs = sb("probs", [P, 2, P])
        y_sb = sb("y_sb", [P, 2, P])
        t_sb = sb("t_sb", [P, 2, P])
        t_hi = sb("t_hi", [P, 2, P], F32R)
        t_lo = sb("t_lo", [P, 2, P], F32R)
        w_sb = sb("w_sb", [P, 8, P])
        wu_hi = sb("wu_hi", [P, 2, P], F32R)
        wu_lo = sb("wu_lo", [P, 2, P], F32R)
        warm = sb("warm", [P, P], mybir.dt.bfloat16)
        ident = sb("ident", [P, P])
        ident2 = sb("ident2", [P, 2, P])
        head_mask = sb("head_mask", [P, P])

        xt_ps = psum("xt_ps", [P, N])
        gt_ps = psum("gt_ps", [P, N])
        out_ps = psum("out_ps", [P, N])
        gu_ps = psum("gu_ps", [P, BANK])
        sy_ps = psum("sy_ps", [P, BANK])
        gram_ps = gu_ps[:, 0:P]
        uv_ps = gu_ps[:, P:3 * P]
        s_ps = sy_ps[:, 0:2 * P]
        t_ps = sy_ps[:, 0:2 * P]
        y_ps = sy_ps[:, 2 * P:4 * P]

        x_loaded = [sem(f"x_loaded{s}") for s in range(SLOTS)]
        g_loaded = [sem(f"g_loaded{s}") for s in range(SLOTS)]
        out_stored = [sem(f"out_stored{s}") for s in range(OUT_SLOTS)]
        x_first_loaded = sem("x_first_loaded")
        g_first_loaded = sem("g_first_loaded")
        last_stored = [sem(f"last_stored{half}") for half in range(2)]
        w_loaded = sem("w_loaded")
        wu_loaded = sem("wu_loaded")
        warm_ready = sem("warm_ready")
        wu_hi_ready = sem("wu_hi_ready")
        wu_lo_ready = sem("wu_lo_ready")
        ident_ready = sem("ident_ready")
        ident2_ready = sem("ident2_ready")
        mask_ready = sem("mask_ready")
        xt_done = sem("xt_done")
        gt_done = sem("gt_done")
        xt_copied = sem("xt_copied")
        gt_copied = sem("gt_copied")
        gram_done = sem("gram_done")
        gram_hi_ready = sem("gram_hi_ready")
        gram_lo_ready = sem("gram_lo_ready")
        uv_done = sem("uv_done")
        uv_copied = sem("uv_copied")
        s_done = sem("s_done")
        s_masked = sem("s_masked")
        exp_done = sem("exp_done")
        inv_done = sem("inv_done")
        probs_ready = sem("probs_ready")
        y_done = sem("y_done")
        y_copied = sem("y_copied")
        t_done = sem("t_done")
        t_summed = sem("t_summed")
        t_hi_ready = sem("t_hi_ready")
        t_lo_ready = sem("t_lo_ready")
        hi_ready = sem("hi_ready")
        lo_ready = sem("lo_ready")
        half_done = sem("half_done")
        half_copied = sem("half_copied")

        block = stack.enter_context(nc.Block())

        def steps(eng, step, first, last):
            whole = range(SLOTS, last + 1 - (last + 1) % SLOTS)
            for i in range(first, whole.start):
                step(i, i % SLOTS, i // SLOTS, i)
            with eng.Fori(whole.start // SLOTS, whole.stop // SLOTS) as t:
                for slot in range(SLOTS):
                    step(t * SLOTS + slot, slot, t, SLOTS + slot)
            for i in range(whole.stop, last + 1):
                step(i, i % SLOTS, i // SLOTS, i)

        @block.gpsimd
        def _(pool):
            nc.gpsimd.memset(ident[:, :], 0.0).then_inc(ident_ready, 1)
            pool.wait_ge(ident_ready, 1)
            nc.gpsimd.affine_select(out=ident[:, :], in_=ident[:, :], compare_op=ALU.not_equal, fill=1.0, base=0,
                                    pattern=[[-1, P]], channel_multiplier=1).then_inc(ident_ready, 1)
            nc.gpsimd.memset(head_mask[:, :], 0.0).then_inc(mask_ready, 1)
            pool.wait_ge(mask_ready, 1)
            mask = head_mask[:, :].rearrange("p (h d) -> p h d", h=HEADS)
            nc.gpsimd.affine_select(out=mask, in_=mask, compare_op=ALU.is_ge, fill=OFF_HEAD, base=0,
                                    pattern=[[-D, HEADS], [0, D]], channel_multiplier=1).then_inc(mask_ready, 1)
            pool.wait_ge(mask_ready, 2)
            nc.gpsimd.affine_select(out=mask, in_=mask, compare_op=ALU.is_ge, fill=OFF_HEAD, base=D - 1,
                                    pattern=[[D, HEADS], [0, D]], channel_multiplier=-1).then_inc(mask_ready, 1)
            pool.wait_ge(ident_ready, 2)
            nc.gpsimd.tensor_copy(ident2[:, 0, :], ident[:, :]).then_inc(ident2_ready, 1)
            nc.gpsimd.tensor_copy(ident2[:, 1, :], ident[:, :]).then_inc(ident2_ready, 1)

        @block.sync
        def _(sp):
            def load(b, slot):
                sp.dma_start(x_raw[:, slot, :], x[b]).then_inc(x_loaded[slot], 16)
                sp.dma_start(g_raw[:, slot, :], ctx[b]).then_inc(g_loaded[slot], 16)

            def store(b, slot):
                sp.wait_ge(half_copied, 2 * b + 2)
                sp.dma_start(out[b], out_sb[:, slot % OUT_SLOTS, :]).then_inc(out_stored[slot % OUT_SLOTS], 16)

            def reload(i, slot):
                sp.wait_ge(xt_done, 2 * i + 2)
                sp.wait_ge(gt_done, 2 * i + 2)
                sp.wait_ge(lo_ready, 2 * i + 2)
                load(i + SLOTS, slot)

            def step(i, slot, visit, i_min):
                reload(i, slot)
                if i_min >= 2:
                    store(i - 2, slot)

            first, second = slice(0, HALF), slice(HALF, N)
            sp.dma_start(x_raw[:, 0, first], x[0][:, first]).then_inc(x_first_loaded, 16)
            sp.dma_start(g_raw[:, 0, first], ctx[0][:, first]).then_inc(g_first_loaded, 16)
            sp.dma_start(x_raw[:, 0, second], x[0][:, second]).then_inc(x_loaded[0], 16)
            sp.dma_start(g_raw[:, 0, second], ctx[0][:, second]).then_inc(g_loaded[0], 16)
            sp.dma_start(w_sb[:, WQR:WKR + 1, :], weights[:, WQR:WKR + 1, :]).then_inc(wu_loaded, 16)
            load(1, 1)
            sp.dma_start(w_sb[:, WKP:, :], weights[:, WKP:, :]).then_inc(w_loaded, 16)
            for b in range(2, SLOTS):
                load(b, b)
            steps(sp, step, 0, B - SLOTS - 1)
            for b in range(B - SLOTS - 2, B - 1):
                store(b, b % SLOTS)
            for half in range(2):
                sp.wait_ge(half_copied, 2 * B - 1 + half)
                cols = slice(half * HALF, (half + 1) * HALF)
                sp.dma_start(out[B - 1][:, cols], out_sb[:, (B - 1) % OUT_SLOTS, cols]).then_inc(last_stored[half], 16)
            sp.wait_ge(out_stored[B % OUT_SLOTS], 16 * (B // OUT_SLOTS))
            sp.wait_ge(out_stored[(B - 1) % OUT_SLOTS], 16 * (B // OUT_SLOTS - 1))
            for half in range(2):
                sp.wait_ge(last_stored[half], 16)

        @block.tensor
        def _(pe):
            pe.wait_ge(warm_ready, 1)
            for _ in range(WARM):
                nc.tensor.matmul(out_ps[:, 0:P], warm[:, :], warm[:, :], start=True, stop=True)
            pe.wait_ge(ident_ready, 2)

            def turn(i, visit, i_min, half, raw, slot, first_loaded, loaded, ps, done, copied):
                if i_min == 0 and half == 0:
                    pe.wait_ge(first_loaded, 16)
                else:
                    pe.wait_ge(loaded[slot], 16 * visit + 16)
                if i_min >= 1:
                    pe.wait_ge(copied, 2 * i - 1 + half)
                for t in range(half * TILES // 2, (half + 1) * TILES // 2):
                    cols = slice(t * TILE, (t + 1) * TILE)
                    last = nc.tensor.transpose(ps[:, cols], raw[:, slot, cols], ident[:, :])
                last.then_inc(done, 1)

            def gram_half(i, half, i_min):
                pe.wait_ge(xt_copied, 2 * i + 1 + half)
                pe.wait_ge(gt_copied, 2 * i + 1 + half)
                if half == 0 and i_min >= 1:
                    pe.wait_ge(gram_lo_ready, i)
                for t in range(half * TILES // 2, (half + 1) * TILES // 2):
                    cols = slice(t * TILE, (t + 1) * TILE)
                    last = nc.tensor.matmul(gram_ps, xt[:, cols], gt[:, cols], start=(t == 0), stop=(t == TILES - 1))
                if half == 1:
                    last.then_inc(gram_done, 1)

            def last_half(b, slot, half, b_min):
                cols = slice(half * HALF, (half + 1) * HALF)
                if b_min >= 1:
                    pe.wait_ge(half_copied, 2 * b - 1 + half)
                parts = [(t_hi, 0, x_hi), (t_hi, 0, x_lo), (t_hi, 1, g_hi), (t_hi, 1, g_lo), (t_lo, 0, x_hi), (t_lo, 1, g_hi)]
                for n, (w, which, moving) in enumerate(parts):
                    if half == 0 and n == 4:
                        pe.wait_ge(t_lo_ready, b + 1)
                    last = nc.tensor.matmul(out_ps[:, cols], w[:, which, :], moving[:, slot, cols],
                                            start=(n == 0), stop=(n == len(parts) - 1))
                last.then_inc(half_done, 1)

            def step(i, slot, visit, i_min):
                gram_on, small_on, last_on = i_min < B, 1 <= i_min <= B, i_min >= 2
                before = (slot - 2) % SLOTS
                if gram_on:
                    turn(i, visit, i_min, 0, x_raw, slot, x_first_loaded, x_loaded, xt_ps, xt_done, xt_copied)
                    turn(i, visit, i_min, 0, g_raw, slot, g_first_loaded, g_loaded, gt_ps, gt_done, gt_copied)
                if small_on:
                    pe.wait_ge(gram_lo_ready, i)
                    if i_min == 1:
                        pe.wait_ge(wu_lo_ready, 1)
                    else:
                        pe.wait_ge(uv_copied, i - 1)
                    nc.tensor.matmul(uv_ps, gram_hi[:, :], wu_hi[:, :, :], start=True, stop=False)
                    nc.tensor.matmul(uv_ps, gram_hi[:, :], wu_lo[:, :, :], start=False, stop=False)
                    nc.tensor.matmul(uv_ps, gram_lo[:, :], wu_hi[:, :, :], start=False, stop=True).then_inc(uv_done, 1)
                if last_on:
                    pe.wait_ge(y_copied, i - 1)
                    nc.tensor.matmul(t_ps[:, 0:P], y_sb[:, 1, :], w_sb[:, PR, :], start=True, stop=True)
                    nc.tensor.matmul(t_ps[:, P:2 * P], y_sb[:, 0, :], w_sb[:, PP, :], start=True,
                                     stop=True).then_inc(t_done, 1)
                if gram_on:
                    turn(i, visit, i_min, 1, x_raw, slot, x_first_loaded, x_loaded, xt_ps, xt_done, xt_copied)
                    turn(i, visit, i_min, 1, g_raw, slot, g_first_loaded, g_loaded, gt_ps, gt_done, gt_copied)
                if small_on:
                    pe.wait_ge(uv_copied, i)
                    if i_min == 1:
                        pe.wait_ge(w_loaded, 16)
                    if i_min >= 2:
                        pe.wait_ge(t_summed, i - 1)
                    nc.tensor.matmul(s_ps[:, 0:P], uv[:, 0, :], w_sb[:, WKP, :], start=True, stop=True)
                    nc.tensor.matmul(s_ps[:, P:2 * P], w_sb[:, WQP, :], uv[:, 1, :], start=True,
                                     stop=True).then_inc(s_done, 1)
                if gram_on:
                    gram_half(i, 0, i_min)
                if last_on:
                    pe.wait_ge(t_hi_ready, i - 1)
                    pe.wait_ge(lo_ready, 2 * i - 2)
                    last_half(i - 2, before, 0, i_min - 2)
                if gram_on:
                    gram_half(i, 1, i_min)
                if small_on:
                    if i_min >= 2:
                        pe.wait_ge(y_copied, i - 1)
                    for a, wv in enumerate((WVP, WVR)):
                        pe.wait_ge(probs_ready, 2 * i - 1 + a)
                        last = nc.tensor.matmul(y_ps[:, a * P:(a + 1) * P], probs[:, a, :], w_sb[:, wv, :],
                                                start=True, stop=True)
                    last.then_inc(y_done, 1)
                if last_on:
                    last_half(i - 2, before, 1, i_min - 2)

            steps(pe, step, 0, B + 1)

        @block.scalar
        def _(act):
            def copy_xt(i, half, i_min):
                act.wait_ge(xt_done, 2 * i + 1 + half)
                if i_min >= 1:
                    act.wait_ge(gram_done, i)
                cols = slice(half * HALF, (half + 1) * HALF)
                nc.scalar.copy(xt[:, cols], xt_ps[:, cols]).then_inc(xt_copied, 1)

            def split_hi(b, slot, b_min, raw, hi):
                act.wait_ge(xt_done, 2 * b + 2)
                act.wait_ge(gt_done, 2 * b + 2)
                if b_min >= SLOTS:
                    act.wait_ge(half_done, 2 * b - 6)
                nc.scalar.copy(hi[:, slot, :], raw[:, slot, :]).then_inc(hi_ready, 1)

            def step(i, slot, visit, i_min):
                gram_on, small_on, last_on = i_min < B, 1 <= i_min <= B, i_min >= 2
                if gram_on:
                    copy_xt(i, 0, i_min)
                if gram_on and small_on:
                    act.wait_ge(uv_done, i)
                    if i_min >= 2:
                        act.wait_ge(s_done, i - 1)
                    nc.scalar.copy(uv[:, :, :], uv_ps.rearrange("p (a c) -> p a c", a=2)).then_inc(uv_copied, 1)
                if gram_on and last_on:
                    act.wait_ge(t_summed, i - 1)
                    if i_min >= 3:
                        act.wait_ge(half_done, 2 * i - 4)
                    nc.scalar.copy(t_hi[:, :, :], t_sb[:, :, :]).then_inc(t_hi_ready, 1)
                if gram_on:
                    copy_xt(i, 1, i_min)
                if i_min == 0:
                    act.wait_ge(wu_loaded, 16)
                    nc.scalar.copy(wu_hi[:, :, :], w_sb[:, WQR:WKR + 1, :]).then_inc(wu_hi_ready, 1)
                if small_on:
                    if i_min >= 2:
                        act.wait_ge(probs_ready, 2 * i - 2)
                    for a in range(2):
                        act.wait_ge(s_masked, 2 * i - 1 + a)
                        nc.scalar.activation(expd[:, a, :], scores[:, a, :], ACT.Exp, bias=min_neg[:, a:a + 1], scale=-1.0,
                                             accum_out=row_sum[:, a:a + 1]).then_inc(exp_done, 1)
                if small_on:
                    before = (slot - 1) % SLOTS
                    split_hi(i - 1, before, i_min - 1, x_raw, x_hi)
                    split_hi(i - 1, before, i_min - 1, g_raw, g_hi)
                if gram_on:
                    act.wait_ge(gram_done, i + 1)
                    if i_min >= 1:
                        act.wait_ge(uv_done, i)
                    nc.scalar.copy(gram_hi[:, :], gram_ps).then_inc(gram_hi_ready, 1)
                if last_on:
                    for half in range(2):
                        act.wait_ge(half_done, 2 * i - 3 + half)
                        if half == 0 and i_min >= 4:
                            act.wait_ge(out_stored[slot % OUT_SLOTS], 16 * (visit * 2 + slot // 2 - 1))
                        cols = slice(half * HALF, (half + 1) * HALF)
                        nc.scalar.copy(out_sb[:, slot % OUT_SLOTS, cols], out_ps[:, cols]).then_inc(half_copied, 1)

            steps(act, step, 0, B + 1)

        @block.vector
        def _(dve):
            def copy_gt(i, half, i_min):
                dve.wait_ge(gt_done, 2 * i + 1 + half)
                if i_min >= 1:
                    dve.wait_ge(gram_done, i)
                cols = slice(half * HALF, (half + 1) * HALF)
                nc.vector.tensor_copy(gt[:, cols], gt_ps[:, cols]).then_inc(gt_copied, 1)

            def split_lo(b, slot, raw, hi, lo, which):
                dve.wait_ge(hi_ready, 2 * b + 1 + which)
                nc.vector.tensor_tensor(lo[:, slot, :], raw[:, slot, :], hi[:, slot, :].bitcast(F32),
                                        ALU.subtract).then_inc(lo_ready, 1)

            nc.vector.memset(warm[:, :], 0.0).then_inc(warm_ready, 1)
            dve.wait_ge(ident2_ready, 2)

            def step(i, slot, visit, i_min):
                gram_on, small_on, last_on = i_min < B, 1 <= i_min <= B, i_min >= 2
                if gram_on:
                    copy_gt(i, 0, i_min)
                if small_on and not gram_on:
                    dve.wait_ge(uv_done, i)
                    dve.wait_ge(s_done, i - 1)
                    nc.vector.tensor_copy(uv[:, :, :], uv_ps.rearrange("p (a c) -> p a c", a=2)).then_inc(uv_copied, 1)
                if last_on:
                    dve.wait_ge(t_done, i - 1)
                    t_in = t_ps.rearrange("p (a c) -> p a c", a=2)
                    if not gram_on:
                        dve.wait_ge(half_done, 2 * i - 4)
                        nc.vector.tensor_tensor(t_hi[:, :, :], t_in, ident2[:, :, :], ALU.add).then_inc(t_hi_ready, 1)
                    if i_min >= 3:
                        dve.wait_ge(t_lo_ready, i - 2)
                    nc.vector.tensor_tensor(t_sb[:, :, :], t_in, ident2[:, :, :], ALU.add).then_inc(t_summed, 1)
                if gram_on:
                    copy_gt(i, 1, i_min)
                if last_on:
                    dve.wait_ge(t_hi_ready, i - 1)
                    if not gram_on:
                        dve.wait_ge(t_summed, i - 1)
                    if i_min >= 3:
                        dve.wait_ge(half_done, 2 * i - 4)
                    nc.vector.tensor_tensor(t_lo[:, :, :], t_sb[:, :, :], t_hi[:, :, :].bitcast(F32),
                                            ALU.subtract).then_inc(t_lo_ready, 1)
                if small_on:
                    dve.wait_ge(mask_ready, 3)
                    dve.wait_ge(s_done, i)
                    for a in range(2):
                        nc.vector.tensor_tensor_reduce(out=scores[:, a, :], in0=s_ps[:, a * P:(a + 1) * P],
                                                       in1=head_mask[:, :], scale=-SCALE, scalar=3.0e38, op0=ALU.add,
                                                       op1=ALU.min, accum_out=min_neg[:, a:a + 1]).then_inc(s_masked, 1)
                if i_min == 0:
                    dve.wait_ge(wu_hi_ready, 1)
                    nc.vector.tensor_tensor(wu_lo[:, :, :], w_sb[:, WQR:WKR + 1, :], wu_hi[:, :, :].bitcast(F32),
                                            ALU.subtract).then_inc(wu_lo_ready, 1)
                if small_on:
                    dve.wait_ge(exp_done, 2 * i)
                    nc.vector.reciprocal(row_inv[:, :], row_sum[:, :]).then_inc(inv_done, 1)
                    dve.wait_ge(inv_done, i)
                    if i_min >= 2:
                        dve.wait_ge(y_done, i - 1)
                    for a in range(2):
                        nc.vector.tensor_scalar(probs[:, a, :], expd[:, a, :], row_inv[:, a:a + 1], None,
                                                ALU.mult).then_inc(probs_ready, 1)
                    split_lo(i - 1, (slot - 1) % SLOTS, x_raw, x_hi, x_lo, 0)
                if gram_on:
                    dve.wait_ge(gram_hi_ready, i + 1)
                    nc.vector.tensor_tensor(gram_lo[:, :], gram_ps, gram_hi[:, :].bitcast(F32),
                                            ALU.subtract).then_inc(gram_lo_ready, 1)
                if small_on:
                    dve.wait_ge(y_done, i)
                    if i_min >= 2:
                        dve.wait_ge(t_done, i - 1)
                    nc.vector.tensor_copy(y_sb[:, :, :], y_ps.rearrange("p (a c) -> p a c", a=2)).then_inc(y_copied, 1)
                    split_lo(i - 1, (slot - 1) % SLOTS, g_raw, g_hi, g_lo, 1)

            steps(dve, step, 0, B + 1)


def kernel(**inputs):
    import numpy as _np
    import concourse.bacc as _bacc
    from concourse import mybir as _mybir
    from concourse.bass_utils import run_bass_kernel_spmd as _run

    w = {name[len("L0_xattn_"):]: _np.asarray(a) for name, a in inputs.items() if name.startswith("L0_xattn_")}
    packed = [w["wq_rgb"].T, w["wk_rgb"].T, w["wk_point"].T, w["wq_point"].T, w["proj_p2r"].T, w["proj_r2p"].T,
              w["wv_point"], w["wv_rgb"]]
    arrays = {
        "in_x_dram": _np.ascontiguousarray(inputs["x"]),
        "in_ctx_dram": _np.ascontiguousarray(inputs["ctx_4096"]),
        "in_weights_dram": _np.ascontiguousarray(_np.stack(packed, axis=1)),
    }
    nc = _bacc.Bacc("TRN2", target_bir_lowering=False, num_devices=1)
    args = [nc.dram_tensor(name, a.shape, _mybir.dt.from_np(a.dtype), kind="ExternalInput").ap()
            for name, a in arrays.items()]
    out = nc.dram_tensor("out_0_dram", arrays["in_x_dram"].shape, _mybir.dt.float32, kind="ExternalOutput").ap()
    bass_cross_channel_attention(nc, *args, out)
    r = _run(nc, [arrays], core_ids=[0])
    return r.results[0]["out_0_dram"]
```
